# Optimizing a Trainium2 kernel written in Bass

```python
import numpy as np
import jax
import jax.numpy as jnp

def _softmax(x, axis=-1):
    return jax.nn.softmax(x, axis=axis)
def _gelu(x):
    return jax.nn.gelu(x, approximate=True)
def _silu(x):
    return jax.nn.silu(x)
def _sigmoid(x):
    return jax.nn.sigmoid(x)
def _layernorm(x, axis=-1, eps=1e-5):
    m = jnp.mean(x, axis=axis, keepdims=True)
    v = jnp.var(x, axis=axis, keepdims=True)
    return (x - m) / jnp.sqrt(v + eps)
def _scatter_add(tgt, idx, src, axis=0):
    return tgt.at[idx].add(src)
def _segment_sum(src, seg, n):
    return jax.ops.segment_sum(src, seg, n)

kernel_name = 'mk_conv_preact_d2_conv_nchw8_71512b'

def setup_inputs(seed: int = 0):
    np.random.seed(seed)
    _w = jnp.asarray
    def _rec_inputs():
        import jax
        import jax.numpy as jnp
        _gk = jax.random.key(seed)
        x = -9.629e-05 + 1 * jax.random.normal(jax.random.fold_in(_gk, 1), (8, 8, 1024, 1024), jnp.float32)
        return x
    x = _rec_inputs()
    def _L0_conv_setup():
        import jax, jax.numpy as jnp
        import numpy as np
        import math
        B, C_IN, C_OUT = (32, 8, 8)
        H, W = (1024, 1024)
        KH, KW = (3, 3)
        STRIDE = 1
        PAD = 1
        key = jax.random.key(seed)
        k1, k2, k3 = jax.random.split(key, 3)
        stdv = math.sqrt(1.0 / (C_IN * KH * KW))
        x = jax.random.normal(k1, (B, C_IN, H, W), dtype=jnp.float32)
        weight = jax.random.uniform(k2, (C_OUT, C_IN, KH, KW), dtype=jnp.float32, minval=-stdv, maxval=stdv)
        bias = jax.random.uniform(k3, (C_OUT,), dtype=jnp.float32, minval=-stdv, maxval=stdv)
        return {'input': x, 'weight': weight, 'bias': bias}
    _L0_conv_all = _L0_conv_setup()
    _L0_conv_in = {k: v for k, v in _L0_conv_all.items() if k in ('weight', 'bias', )}
    del _L0_conv_all

    def _L1_conv_setup():
        import jax, jax.numpy as jnp
        import numpy as np
        key = jax.random.key(seed)
        k1, k2, k3 = jax.random.split(key, 3)
        x = jax.random.normal(k1, (16, 8, 1024, 1024), dtype=jnp.float32)
        weight = jax.random.normal(k2, (8, 8, 3, 3), dtype=jnp.float32) * 0.1
        bias = jax.random.normal(k3, (8,), dtype=jnp.float32) * 0.1
        return {'x': x, 'weight': weight, 'bias': bias}
    _L1_conv_all = _L1_conv_setup()
    _L1_conv_in = {k: v for k, v in _L1_conv_all.items() if k in ('weight', 'bias', )}
    del _L1_conv_all

    return {
        "x": x,
        "L0_conv_weight": _L0_conv_in["weight"],
        "L0_conv_bias": _L0_conv_in["bias"],
        "L1_conv_weight": _L1_conv_in["weight"],
        "L1_conv_bias": _L1_conv_in["bias"],
    }

def reference(x, L0_conv_weight, L0_conv_bias, L1_conv_weight, L1_conv_bias):
    import jax
    import jax.numpy as jnp
    def _L0_conv_ref(input, weight, bias):
        import jax, jax.numpy as jnp
        import numpy as np
        import math
        B, C_IN, C_OUT = (32, 8, 8)
        H, W = (1024, 1024)
        KH, KW = (3, 3)
        STRIDE = 1
        PAD = 1
        out = jax.lax.conv_general_dilated(input, weight, window_strides=(STRIDE, STRIDE), padding=[(PAD, PAD), (PAD, PAD)], dimension_numbers=('NCHW', 'OIHW', 'NCHW'))
        return out + bias[None, :, None, None]

    def _L1_conv_ref(x, weight, bias):
        import jax, jax.numpy as jnp
        import numpy as np
        out = jax.lax.conv_general_dilated(x, weight, window_strides=(1, 1), padding=((1, 1), (1, 1)), dimension_numbers=('NCHW', 'OIHW', 'NCHW'))
        return out + bias[None, :, None, None]

    def _gn(v, G=4, eps=1e-5):
        B_, C_, H_, W_ = v.shape
        g = v.reshape(B_, G, C_ // G, H_, W_)
        m = jnp.mean(g, axis=(2, 3, 4), keepdims=True)
        s = jnp.var(g, axis=(2, 3, 4), keepdims=True)
        return ((g - m) / jnp.sqrt(s + eps)).reshape(v.shape)

    def _ln_c(v, eps=1e-6):
        m = jnp.mean(v, axis=1, keepdims=True)
        s = jnp.var(v, axis=1, keepdims=True)
        return (v - m) / jnp.sqrt(s + eps)

    def _ln_t(v, eps=1e-5):
        m = jnp.mean(v, axis=-1, keepdims=True)
        s = jnp.var(v, axis=-1, keepdims=True)
        return (v - m) / jnp.sqrt(s + eps)

    def _to_tokens(v):
        B_, C_, H_, W_ = v.shape
        return v.reshape(B_, C_, H_ * W_).transpose(0, 2, 1)
    def _from_tokens(t, like):
        B_, C_, H_, W_ = like.shape
        return t.transpose(0, 2, 1).reshape(B_, C_, H_, W_)

    x = x + _L0_conv_ref(_gn(x), L0_conv_weight, L0_conv_bias)
    x = x + _L1_conv_ref(_gn(x), L1_conv_weight, L1_conv_bias)
    return x


_drawn_inputs = setup_inputs


def setup_inputs(seed=0):
    import zlib

    import numpy as np

    out = dict(_drawn_inputs(seed))
    spreads = {}
    factors = {}
    for name, (base, spread) in spreads.items():
        noise = np.random.default_rng([zlib.crc32(name.encode()), seed]).standard_normal(out[name].shape)
        drawn = base * np.exp(spread * noise) if base else spread * noise
        out[name] = jnp.asarray(drawn.astype(out[name].dtype))
    for name, factor in factors.items():
        out[name] = (out[name] * factor).astype(out[name].dtype)
    return out
```

```python
from contextlib import ExitStack

import concourse.bass as bass
from concourse import mybir

F32 = mybir.dt.float32
F32R = mybir.dt.float32r
BF16 = mybir.dt.bfloat16
ALU = mybir.AluOpType
ACT = mybir.ActivationFunctionType
AX_X = mybir.AxisListType.X

P = 128
CH = 8
IMAGES = 8
SIDE = 1024
ROWS = P // CH
STEP = ROWS - 2
TILES = (SIDE - ROWS) // STEP + 1
GROUP_CH = 2
GROUP_SIZE = GROUP_CH * SIDE * SIDE
EPS = 1e-5
BANK = 512
HALVES = SIDE // BANK
KW = 3

RING = 4
LAST = TILES - 1
HEAD = RING + 1
TRIPS = 16
TAIL = HEAD + TRIPS * RING
PARTS = 2
LAG = 3
X_TILES = SIDE // ROWS
X_SLOTS = 8
WINDOWS = 2 * IMAGES
PAIRS = IMAGES - 2

XPREP, SUMS, BAND = 9, 10, 3

assert LAST % RING == 0 and LAST % PARTS == 0 and (SIDE - ROWS) % STEP == 0 and TAIL < LAST - 2


class Tile:

    def __init__(self, n0, k=0):
        self.n = k * RING + n0
        self.last = n0 == LAST
        self.slot = RING if self.last else n0 % RING
        self.part = PARTS if self.last else n0 % PARTS
        self.turn = 0 if self.last else k + n0 // RING


class Window:

    def __init__(self, w, layer, image, parity, x_image=None, x_each=0, x_first=0, x_before=0,
                 x_uses=0):
        self.w, self.layer, self.image, self.parity = w, layer, image, parity
        self.x_image, self.x_each, self.x_first = x_image, x_each, x_first
        self.x_before, self.x_uses = x_before, x_uses

    def count(self, n):
        return self.w * TILES + n

    def uses(self, tile):
        return self.w * (1 if tile.last else LAST // RING) + tile.turn


FIRST = Window(0, 0, 0, 0, x_image=1, x_each=4, x_before=X_TILES, x_uses=X_TILES // X_SLOTS)


def pair(i):
    uses = FIRST.x_uses + TRIPS + i * (2 * TRIPS)
    before = (i + 2) * X_TILES
    return (Window(i * 2 + 1, 0, i + 1, 1, i + 2, 2, 0, before, uses),
            Window(i * 2 + 2, 1, i, 0, i + 2, 2, X_TILES // 2, before + X_TILES // 2,
                   uses + TRIPS))


CLOSING = (Window(WINDOWS - 3, 0, IMAGES - 1, 1), Window(WINDOWS - 2, 1, IMAGES - 2, 0),
           Window(WINDOWS - 1, 1, IMAGES - 1, 1))


def in_order(engine, step):
    for n in range(HEAD):
        step(Tile(n), None)
    with engine.Fori(0, TRIPS) as k:
        for j in range(RING):
            step(Tile(HEAD + j, k), (j, k))
    for n in range(TAIL, TILES):
        step(Tile(n), None)


def conv_preact_blocks(nc: bass.Bass, x: bass.AP, taps: bass.AP, bias: bass.AP,
                       group_sums: bass.AP, out: bass.AP):
    mid = nc.dram_tensor("mid_dram", (IMAGES, SIDE * CH, SIDE), F32).ap()

    with ExitStack() as ctx:
        def sb(name, shape, dt=F32):
            return ctx.enter_context(nc.sbuf_tensor(name, shape, dt))

        def sem(name):
            return ctx.enter_context(nc.semaphore(name))

        x_tile = sb("x_tile", [P, RING + 1, SIDE])
        out_tile = sb("out_tile", [P, RING + 1, SIDE])
        high = sb("high", [P, PARTS + 1, SIDE + 2], F32R)
        low = sb("low", [P, PARTS + 1, SIDE + 2], F32R)
        stat_tile = sb("stat_tile", [P, X_SLOTS, SIDE])
        unread = sb("unread", [P, RING + 1, 2, SIDE], BF16)
        carrier = sb("carrier", [P, 3])
        band = sb("band", [P, 2, KW, P])
        scaled = sb("scaled", [P, KW, P])
        band_high = sb("band_high", [P, 2, KW, P], F32R)
        band_low = sb("band_low", [P, 2, KW, P], F32R)
        sums_of = sb("sums_of", [P, 4, P])
        ALL, INNER, TOP, BOTTOM = range(4)
        bias_col = sb("bias_col", [P, 2])
        minus_mean = sb("minus_mean", [P, 2])
        next_minus_mean = sb("next_minus_mean", [P, 1])
        rstd_x = sb("rstd_x", [P, 1])
        rstd_mid = sb("rstd_mid", [P, 1])
        bn = sb("bn", [P, X_TILES * HALVES, 6])
        bn_mean_var = sb("bn_mean_var", [P, 2])
        tile_sums = sb("tile_sums", [P, 2, TILES])
        total = sb("total", [P, 2])
        shift, moment, var_x, root_x, newton_x = (sb(n, [P, 1]) for n in (
            "shift", "moment", "var_x", "root_x", "newton_x"))
        moments_mid, var_mid, root_mid, newton_mid = (sb(n, [P, k]) for n, k in (
            ("moments_mid", 2), ("var_mid", 1), ("root_mid", 1), ("newton_mid", 1)))
        conv = ctx.enter_context(nc.psum_tensor("conv", [P, PARTS + 1, SIDE], F32))
        group_x = ctx.enter_context(nc.psum_tensor("group_x", [P, BANK], F32))
        group_mid = ctx.enter_context(nc.psum_tensor("group_mid", [P, BANK], F32))

        setup_loaded = sem("setup_loaded")
        SETUP = 16 * (2 * ROWS + 2)
        band_zeroed, pads_zeroed = sem("band_zeroed"), sem("pads_zeroed")
        x_loaded = [sem(f"x_loaded{s}") for s in range(RING + 1)]
        stored = [sem(f"stored{s}") for s in range(RING + 1)]
        stat_loaded = [sem(f"stat_loaded{s}") for s in range(X_SLOTS)]
        stat_used = sem("stat_used")
        high_ready = sem("high_ready")
        low_ready = sem("low_ready")
        conv_done = sem("conv_done")
        out_ready = sem("out_ready")
        sums_taken = sem("sums_taken")
        xprep_v, xprep_p, xprep_a = sem("xprep_v"), sem("xprep_p"), sem("xprep_a")
        sums_v, sums_p, sums_a = sem("sums_v"), sem("sums_p"), sem("sums_a")
        band_v = sem("band_v")

        def rows_of(src, image, row, rows):
            if src is mid:
                return mid[image, bass.ds(row * CH, rows * CH), :]
            return src[image, :, bass.ds(row, rows), :].rearrange("c r w -> r c w")

        block = ctx.enter_context(nc.Block())

        @block.sync
        def _(sp):
            def load_stat(image, q, s, used=None):
                if used is not None:
                    sp.wait_ge(stat_used, used)
                sp.dma_start(stat_tile[:, s], rows_of(x, image, q * ROWS, ROWS))                   .then_inc(stat_loaded[s], 16)

            def load(win, tile):
                sp.dma_start(x_tile[:, tile.slot],
                             rows_of(mid if win.layer else x, win.image, tile.n * STEP, ROWS))                   .then_inc(x_loaded[tile.slot], 16)

            def store(win, tile):
                first = 0 if isinstance(tile.n, int) and tile.n == 0 else 1
                end = ROWS if tile.last else ROWS - 1
                sp.dma_start(rows_of(out if win.layer else mid, win.image, tile.n * STEP + first,
                                     end - first),
                             out_tile[CH * first:CH * end, tile.slot])                   .then_inc(stored[tile.slot], 16)

            def wait_for_result(count):
                sp.wait_ge(out_ready, count + 1)

            def window(win, following):
                def step(tile, in_loop):
                    if not in_loop and tile.n < RING:
                        return
                    wait_for_result(win.count(tile.n) - RING)
                    if in_loop:
                        j, k = in_loop
                        store(win, Tile(HEAD + j - RING, k))
                        load(win, tile)
                        if j < win.x_each:
                            q = k * win.x_each + j
                            load_stat(win.x_image, q + win.x_first, j,
                                      win.x_before - win.x_each + 1 + q)
                    else:
                        store(win, Tile(tile.n - RING))
                        load(win, tile)

                in_order(sp, step)
                for n in range(RING):
                    wait_for_result(win.count(TILES - RING + n))
                    store(win, Tile(TILES - RING + n))
                    if following:
                        load(following, Tile(n))

            for s in range(X_SLOTS):
                load_stat(0, s, s)
            with sp.Fori(1, X_TILES // X_SLOTS) as k:
                for s in range(X_SLOTS):
                    load_stat(0, k * X_SLOTS + s, s, k * X_SLOTS + (s + 1 - X_SLOTS))
            for n in range(RING):
                load(FIRST, Tile(n))
            window(FIRST, pair(0)[0])
            with sp.Fori(0, PAIRS) as i:
                layer0, layer1 = pair(i)
                window(layer0, layer1)
                window(layer1, pair(i + 1)[0])
            for win, following in zip(CLOSING, (*CLOSING[1:], None)):
                window(win, following)
            for s in range(RING):
                sp.wait_ge(stored[s], WINDOWS * 16 * (LAST // RING))
            sp.wait_ge(stored[RING], WINDOWS * 16)

        @block.scalar
        def _(act):
            act.wait_ge(band_zeroed, 1)
            for layer in range(2):
                for r in range(ROWS):
                    lo, hi = max(r - 1, 0), min(r + 2, ROWS)
                    act.dma_start(band[CH * r:CH * (r + 1), layer, :, CH * lo:CH * hi],
                                  taps[layer, :, :, CH * (lo - r + 1):CH * (hi - r + 1)]) \
                       .then_inc(setup_loaded, 16)
            act.dma_start(bias_col[:, :], bias).then_inc(setup_loaded, 16)
            act.dma_start(sums_of[:, :, :], group_sums).then_inc(setup_loaded, 16)

            def split(win, tile):
                count = win.count(tile.n)
                act.wait_ge(x_loaded[tile.slot], (win.uses(tile) + 1) * 16)
                if not isinstance(count, int) or count >= PARTS:
                    act.wait_ge(conv_done, count - PARTS + 1)
                act.activation(high[:, tile.part, 1:SIDE + 1], x_tile[:, tile.slot], ACT.Identity,
                               bias=minus_mean[:, win.parity:win.parity + 1]).then_inc(high_ready, 1)

            def take_sums(win, tile):
                for power, func in enumerate((ACT.Identity, ACT.Square)):
                    last = act.activation(unread[:, tile.slot, power], out_tile[:, tile.slot], func,
                                          bias=minus_mean[:, win.parity:win.parity + 1],
                                          accum_out=tile_sums[:, power, bass.ds(tile.n, 1)])
                last.then_inc(sums_taken, 1)

            def root(to, of, steps, count, done):
                act.wait_ge(steps, count)
                act.activation(to[:, :], of[:, :], ACT.Sqrt).then_inc(done, 1)

            def x_root(j):
                root(root_x, var_x, xprep_v, j * XPREP + 5, xprep_a)

            def mid_root(j):
                root(root_mid, var_mid, sums_v, j * SUMS + 6, sums_a)

            def window(win, before=None, ahead_of={}):
                def step(tile, in_loop):
                    n = tile.n
                    late = None
                    if in_loop:
                        late = win, Tile(HEAD + in_loop[0] - LAG, in_loop[1])
                    elif n >= LAG:
                        late = win, Tile(n - LAG)
                    elif before:
                        late = before, Tile(TILES + n - LAG)
                    if late and late[0].layer:
                        late = None
                    if late:
                        act.wait_ge(out_ready, win.count(n) - LAG + 1)
                    if not in_loop:
                        for prepare in ahead_of.get(n, ()):
                            prepare()
                    split(win, tile)
                    if late:
                        take_sums(*late)

                act.wait_ge(band_v, (win.w + 1) * BAND)
                in_order(act, step)

            x_root(0)
            window(FIRST, ahead_of={LAST: [lambda: x_root(1)]})
            for n in range(TILES - LAG, TILES):
                act.wait_ge(out_ready, FIRST.count(n) + 1)
                take_sums(FIRST, Tile(n))
            mid_root(0)
            with act.Fori(0, PAIRS) as i:
                layer0, layer1 = pair(i)
                window(layer0)
                window(layer1, layer0, {LAST - 1: [lambda: mid_root(i + 1)],
                                        LAST: [lambda: x_root(i + 2)]})
            window(CLOSING[0])
            window(CLOSING[1], CLOSING[0], {LAST - 1: [lambda: mid_root(IMAGES - 1)]})
            window(CLOSING[2])

        @block.tensor
        def _(pe):
            def convolve(win, tile):
                count = win.count(tile.n)
                pe.wait_ge(high_ready, count + 1)
                if not isinstance(count, int) or count >= PARTS:
                    pe.wait_ge(out_ready, count - PARTS + 1)
                products = [(b, high, kw) for kw in range(KW) for b in (band_high, band_low)]
                products += [(band_high, low, kw) for kw in range(KW)]
                for m, (b, part, kw) in enumerate(products):
                    if m == 2 * KW:
                        pe.wait_ge(low_ready, count + 1)
                    for c in range(0, SIDE, BANK):
                        last = nc.tensor.matmul(conv[:, tile.part, c:c + BANK],
                                                b[:, win.parity, kw, :],
                                                part[:, tile.part, c + kw:c + kw + BANK],
                                                start=(m == 0), stop=(m == 3 * KW - 1))
                last.then_inc(conv_done, 1)

            def window(win, ahead_of={}):
                def step(tile, in_loop):
                    if not in_loop:
                        for prepare in ahead_of.get(tile.n, ()):
                            prepare()
                    convolve(win, tile)

                pe.wait_ge(band_v, (win.w + 1) * BAND)
                in_order(pe, step)

            def x_mean(j):
                pe.wait_ge(xprep_v, j * XPREP + 1)
                nc.tensor.matmul(group_x[:, 0:1], sums_of[:, ALL, :], bn_mean_var[:, 0:1],
                                 start=True, stop=True).then_inc(xprep_p, 1)

            def x_variance(j):
                pe.wait_ge(xprep_v, j * XPREP + 4)
                nc.tensor.matmul(group_x[:, 0:1], sums_of[:, ALL, :], moment[:, :],
                                 start=True, stop=True).then_inc(xprep_p, 1)

            def mid_moments(j):
                pe.wait_ge(sums_v, j * SUMS + 1)
                for rows, sums in ((INNER, total[:, :]), (TOP, tile_sums[:, :, 0]),
                                   (BOTTOM, tile_sums[:, :, LAST])):
                    last = nc.tensor.matmul(group_mid[:, 0:2], sums_of[:, rows, :], sums,
                                            start=(rows == INNER), stop=(rows == BOTTOM))
                last.then_inc(sums_p, 1)

            pe.wait_ge(setup_loaded, SETUP)
            pe.wait_ge(pads_zeroed, 2)
            x_mean(0)
            x_variance(0)
            window(FIRST, {TAIL: [lambda: x_mean(1)], TAIL + 1: [lambda: x_variance(1)]})
            mid_moments(0)
            with pe.Fori(0, PAIRS) as i:
                layer0, layer1 = pair(i)
                window(layer0)
                window(layer1, {TAIL: [lambda: mid_moments(i + 1), lambda: x_mean(i + 2)],
                                TAIL + 1: [lambda: x_variance(i + 2)]})
            window(CLOSING[0])
            window(CLOSING[1], {TAIL: [lambda: mid_moments(IMAGES - 1)]})
            window(CLOSING[2])

        @block.vector
        def _(dve):
            def take_stats(q, s):
                for c in range(HALVES):
                    last = dve.bn_stats(
                        bn[:, bass.ds(q * HALVES + c, 1), :].rearrange("p a b -> p (a b)"),
                        stat_tile[:, s, c * BANK:(c + 1) * BANK])
                last.then_inc(stat_used, 1)

            def split(win, tile):
                dve.wait_ge(high_ready, win.count(tile.n) + 1)
                dve.scalar_tensor_tensor(low[:, tile.part, 1:SIDE + 1], x_tile[:, tile.slot],
                                         minus_mean[:, win.parity:win.parity + 1],
                                         high[:, tile.part, 1:SIDE + 1].bitcast(F32),
                                         ALU.add, ALU.subtract).then_inc(low_ready, 1)

            def add_up(win, tile, sums=None):
                uses = win.uses(tile)
                dve.wait_ge(conv_done, win.count(tile.n) + 1)
                if not isinstance(uses, int) or uses:
                    dve.wait_ge(stored[tile.slot], uses * 16)
                if sums is not None:
                    dve.wait_ge(sums_taken, sums)
                dve.scalar_tensor_tensor(out_tile[:, tile.slot], conv[:, tile.part, :],
                                         bias_col[:, win.layer:win.layer + 1],
                                         x_tile[:, tile.slot],
                                         ALU.add, ALU.add).then_inc(out_ready, 1)

            def sums_before(win, tile):
                if isinstance(tile.n, int) and tile.n < RING:
                    after_layer0 = win.layer == 1 and win is not CLOSING[2]
                    return (win.image + 1) * TILES + (LAST - RING + tile.n + 1) if after_layer0 \
                        else None
                return win.image * TILES + tile.n - RING + 1 if win.layer == 0 and not tile.last \
                    else None

            def window(win, following, ahead_of={}):
                def step(tile, in_loop):
                    n = tile.n
                    if not in_loop:
                        for prepare in ahead_of.get(n, ()):
                            prepare()
                        if n:
                            split(win, tile)
                            add_up(win, Tile(n - 1), sums_before(win, Tile(n - 1)))
                        return
                    j, k = in_loop
                    if j < win.x_each:
                        dve.wait_ge(stat_loaded[j], (win.x_uses + 1 + k) * 16)
                    split(win, tile)
                    if j < win.x_each:
                        take_stats(k * win.x_each + (win.x_first + j), j)
                    late = Tile(HEAD + j - 1, k)
                    add_up(win, late, sums_before(win, late))

                in_order(dve, step)
                if following:
                    split(following, Tile(0))
                add_up(win, Tile(LAST))

            def rstd(to, root, var, newton, steps, count):
                dve.reciprocal(to[:, :], root[:, :]).then_inc(steps, 1)
                dve.wait_ge(steps, count + 1)
                dve.scalar_tensor_tensor(newton[:, :], to[:, :], to[:, :], var[:, :],
                                         ALU.mult, ALU.mult).then_inc(steps, 1)
                dve.wait_ge(steps, count + 2)
                dve.tensor_scalar(newton[:, :], newton[:, :], -0.5, 1.5, ALU.mult, ALU.add) \
                   .then_inc(steps, 1)
                dve.wait_ge(steps, count + 3)
                dve.tensor_tensor(to[:, :], to[:, :], newton[:, :], ALU.mult).then_inc(steps, 1)

            def x_means(j):
                dve.wait_ge(stat_used, (j + 1) * X_TILES)
                dve.memset(carrier[:, 2:3], 0.0)
                dve.bn_aggr(bn_mean_var[:, :], bn[:, :, :].rearrange("p a b -> p (a b)")) \
                   .then_inc(xprep_v, 1)

            def x_moments(j, parity):
                mean = minus_mean[:, parity:parity + 1]
                dve.wait_ge(xprep_p, j * 2 + 1)
                dve.tensor_scalar(mean, group_x[:, 0:1], -1.0, None, ALU.mult) \
                   .then_inc(xprep_v, 1)
                dve.wait_ge(xprep_v, j * XPREP + 2)
                dve.tensor_tensor(shift[:, :], bn_mean_var[:, 0:1], mean, ALU.add) \
                   .then_inc(xprep_v, 1)
                dve.wait_ge(xprep_v, j * XPREP + 3)
                dve.scalar_tensor_tensor(moment[:, :], shift[:, :], shift[:, :],
                                         bn_mean_var[:, 1:2], ALU.mult, ALU.add) \
                   .then_inc(xprep_v, 1)

            def x_variance(j):
                dve.wait_ge(xprep_p, j * 2 + 2)
                dve.tensor_scalar(var_x[:, :], group_x[:, 0:1], EPS, None, ALU.add) \
                   .then_inc(xprep_v, 1)

            def x_rstd(j):
                dve.wait_ge(xprep_a, j + 1)
                rstd(rstd_x, root_x, var_x, newton_x, xprep_v, j * XPREP + 5)

            def mid_totals(j):
                dve.wait_ge(sums_taken, (j + 1) * TILES)
                dve.tensor_reduce(total[:, :], tile_sums[:, :, :], AX_X, ALU.add) \
                   .then_inc(sums_v, 1)

            def mid_variance(j, parity):
                dve.wait_ge(sums_p, j + 1)
                dve.tensor_copy(moments_mid[:, :], group_mid[:, 0:2]).then_inc(sums_v, 1)
                dve.wait_ge(sums_v, j * SUMS + 2)
                dve.tensor_tensor(next_minus_mean[:, :], minus_mean[:, parity:parity + 1],
                                  moments_mid[:, 0:1], ALU.subtract).then_inc(sums_v, 1)
                dve.scalar_tensor_tensor(var_mid[:, :], moments_mid[:, 0:1], moments_mid[:, 0:1],
                                         moments_mid[:, 1:2], ALU.mult, ALU.subtract) \
                   .then_inc(sums_v, 1)
                dve.wait_ge(sums_v, j * SUMS + 4)
                dve.tensor_scalar(var_mid[:, :], var_mid[:, :], -1.0, 0.0, ALU.mult, ALU.max) \
                   .then_inc(sums_v, 1)
                dve.wait_ge(sums_v, j * SUMS + 5)
                dve.tensor_scalar(var_mid[:, :], var_mid[:, :], EPS, None, ALU.add) \
                   .then_inc(sums_v, 1)

            def mid_rstd(j):
                dve.wait_ge(sums_a, j + 1)
                rstd(rstd_mid, root_mid, var_mid, newton_mid, sums_v, j * SUMS + 6)

            def make_bands(w, layer, parity, by):
                dve.tensor_scalar(scaled[:, :, :], band[:, layer], by[:, 0:1], None, ALU.mult) \
                   .then_inc(band_v, 1)
                dve.wait_ge(band_v, w * BAND + 1)
                dve.tensor_copy(band_high[:, parity], scaled[:, :, :]).then_inc(band_v, 1)
                dve.wait_ge(band_v, w * BAND + 2)
                dve.tensor_tensor(band_low[:, parity], scaled[:, :, :],
                                  band_high[:, parity].bitcast(F32), ALU.subtract) \
                   .then_inc(band_v, 1)

            def layer0_bands(w, j, parity):
                dve.wait_ge(xprep_v, (j + 1) * XPREP)
                make_bands(w, 0, parity, rstd_x)

            def layer1_bands(w, j, parity):
                dve.wait_ge(sums_v, (j + 1) * SUMS)
                dve.tensor_copy(minus_mean[:, parity:parity + 1], next_minus_mean[:, :])
                make_bands(w, 1, parity, rstd_mid)

            dve.memset(band[:, :, :, :], 0.0).then_inc(band_zeroed, 1)
            for part in (high, low):
                dve.memset(part[:, :, 0:SIDE + 2:SIDE + 1].bitcast(F32), 0.0) \
                   .then_inc(pads_zeroed, 1)
            with dve.Fori(0, X_TILES // X_SLOTS) as k:
                for s in range(X_SLOTS):
                    dve.wait_ge(stat_loaded[s], (k + 1) * 16)
                    if s:
                        dve.wait_ge(stat_used, k * X_SLOTS + s)
                    dve.memset(carrier[:, 0:1] if s else carrier[:, 1:2], 0.0)
                    take_stats(k * X_SLOTS + s, s)
            x_means(0)
            x_moments(0, 0)
            x_variance(0)
            x_rstd(0)
            dve.wait_ge(setup_loaded, SETUP)
            layer0_bands(0, 0, 0)
            split(FIRST, Tile(0))
            window(FIRST, None, {TAIL: [lambda: x_means(1)],
                                 TAIL + 1: [lambda: x_moments(1, 1)],
                                 TAIL + 2: [lambda: x_variance(1)],
                                 LAST: [lambda: x_rstd(1), lambda: layer0_bands(1, 1, 1)]})
            mid_totals(0)
            mid_variance(0, 0)
            mid_rstd(0)
            split(pair(0)[0], Tile(0))
            with dve.Fori(0, PAIRS) as i:
                layer0, layer1 = pair(i)
                window(layer0, layer1, {LAST: [lambda: layer1_bands(layer1.w, i, 0)]})
                window(layer1, pair(i + 1)[0], {
                    TAIL: [lambda: mid_totals(i + 1), lambda: x_means(i + 2)],
                    TAIL + 1: [lambda: mid_variance(i + 1, 1), lambda: x_moments(i + 2, 1)],
                    TAIL + 2: [lambda: mid_rstd(i + 1), lambda: x_variance(i + 2)],
                    LAST: [lambda: x_rstd(i + 2), lambda: layer0_bands(layer1.w + 1, i + 2, 1)]})
            layer0, next_to_last, last = CLOSING
            window(layer0, next_to_last,
                   {LAST: [lambda: layer1_bands(next_to_last.w, IMAGES - 2, 0)]})
            window(next_to_last, last, {
                TAIL: [lambda: mid_totals(IMAGES - 1)],
                TAIL + 1: [lambda: mid_variance(IMAGES - 1, 1)],
                TAIL + 2: [lambda: mid_rstd(IMAGES - 1)],
                LAST: [lambda: layer1_bands(last.w, IMAGES - 1, 1)]})
            window(last, None)


def _taps(weight, np):
    return np.transpose(np.asarray(weight)[:, :, ::-1, :], (1, 3, 2, 0)).reshape(CH, KW, -1)


def _group_sums(np):
    channel, row = np.arange(P) % CH, np.arange(P) // CH
    same = (channel[:, None] // GROUP_CH) == (channel[None, :] // GROUP_CH)
    inner = (row >= 1) & (row <= ROWS - 2)
    parts = (same / (ROWS * GROUP_CH), same * inner[:, None] / GROUP_SIZE,
             same * (row == 0)[:, None] / GROUP_SIZE,
             same * (row == ROWS - 1)[:, None] / GROUP_SIZE)
    return np.ascontiguousarray(np.stack(parts, axis=1), dtype=np.float32)


def kernel(x, L0_conv_weight, L0_conv_bias, L1_conv_weight, L1_conv_bias):
    import numpy as np
    import concourse.bacc as bacc
    from concourse.bass_utils import run_bass_kernel_spmd

    biases = np.stack([np.asarray(L0_conv_bias), np.asarray(L1_conv_bias)], axis=1)
    arrays = {
        "x_dram": np.ascontiguousarray(x),
        "taps_dram": np.ascontiguousarray(np.stack([_taps(L0_conv_weight, np),
                                                    _taps(L1_conv_weight, np)])),
        "bias_dram": np.ascontiguousarray(np.tile(biases, (ROWS, 1))),
        "group_sums_dram": _group_sums(np),
    }
    nc = bacc.Bacc("TRN2", target_bir_lowering=False, num_devices=1)
    args = [nc.dram_tensor(name, a.shape, mybir.dt.from_np(a.dtype), kind="ExternalInput").ap()
            for name, a in arrays.items()]
    out = nc.dram_tensor("out_dram", (IMAGES, CH, SIDE, SIDE), F32, kind="ExternalOutput").ap()
    conv_preact_blocks(nc, *args, out)
    result = run_bass_kernel_spmd(nc, [arrays], core_ids=[0])
    return result.results[0]["out_dram"]
```
